# Optimizing a Trainium2 kernel written in Bass

```python
import numpy as np
import jax
import jax.numpy as jnp

def _softmax(x, axis=-1):
    return jax.nn.softmax(x, axis=axis)

def _gelu(x):
    return jax.nn.gelu(x, approximate=True)

def _silu(x):
    return jax.nn.silu(x)

def _sigmoid(x):
    return jax.nn.sigmoid(x)

def _layernorm(x, axis=-1, eps=1e-05):
    m = jnp.mean(x, axis=axis, keepdims=True)
    v = jnp.var(x, axis=axis, keepdims=True)
    return (x - m) / jnp.sqrt(v + eps)

def _scatter_add(tgt, idx, src, axis=0):
    return tgt.at[idx].add(src)

def _segment_sum(src, seg, n):
    return jax.ops.segment_sum(src, seg, n)
kernel_name = 'mk_cond_resid_d2_seqx_r2_6e4bb0'

def setup_inputs(seed: int=0):
    np.random.seed(seed)
    _w = jnp.asarray

    def _rec_inputs():
        import jax
        import jax.numpy as jnp
        _rk = jax.random.key(seed)
        x = -1.528e-05 + 0.9999 * jax.random.normal(jax.random.fold_in(_rk, 1), (128, 128, 512), jnp.float32)
        _lenS = 128 - jax.random.randint(jax.random.fold_in(_rk, 7), (128,), 0, max(1, 128 // 4) + 1, jnp.int32)
        _lenS2 = 128 - jax.random.randint(jax.random.fold_in(_rk, 8), (128,), 0, max(1, 128 // 4) + 1, jnp.int32)
        cond_1024 = -0.00608245 + 1.00131 * jax.random.normal(jax.random.fold_in(_rk, 11), (128, 512), jnp.float32)
        return (x, cond_1024)
    x, cond_1024 = _rec_inputs()

    def _L0_cond_setup():
        import jax, jax.numpy as jnp
        import numpy as np
        LATENT = 512
        key = jax.random.key(seed)
        k1, k2, k3, k4 = jax.random.split(key, 4)
        B, T, D = (64, 256, LATENT)
        h_t = jax.random.normal(k1, (B, D), dtype=jnp.float32)
        z = jax.random.normal(k2, (B, T, D), dtype=jnp.float32)
        bound = 1.0 / np.sqrt(2 * D)
        W = jax.random.uniform(k3, (D, 2 * D), minval=-bound, maxval=bound, dtype=jnp.float32)
        b = jax.random.uniform(k4, (D,), minval=-bound, maxval=bound, dtype=jnp.float32)
        alpha = jnp.full((D,), 0.1, dtype=jnp.float32)
        return {'h_t': h_t, 'z': z, 'W': W, 'b': b, 'alpha': alpha}
    _L0_cond_all = _L0_cond_setup()
    _L0_cond_in = {k: v for k, v in _L0_cond_all.items() if k in ('W', 'b', 'alpha')}
    del _L0_cond_all

    def _L1_cond_setup():
        import jax, jax.numpy as jnp
        import numpy as np
        N, T, D, H = (64, 256, 512, 512)
        key = jax.random.key(seed)
        k1, k2, k3, k4 = jax.random.split(key, 4)
        x = jax.random.normal(k1, (N, T, D), dtype=jnp.float32)
        h0 = jax.random.normal(k2, (N, H), dtype=jnp.float32)
        Wx = jax.random.normal(k3, (D, H), dtype=jnp.float32) / jnp.sqrt(jnp.float32(D))
        Wh = jax.random.normal(k4, (H, H), dtype=jnp.float32) / jnp.sqrt(jnp.float32(H))
        b = jnp.zeros((H,), dtype=jnp.float32)
        return {'x': x, 'h0': h0, 'Wx': Wx, 'Wh': Wh, 'b': b}
    _L1_cond_all = _L1_cond_setup()
    _L1_cond_in = {k: v for k, v in _L1_cond_all.items() if k in ('Wx', 'Wh', 'b')}
    del _L1_cond_all
    return {'x': x, 'cond_1024': cond_1024, 'L0_cond_W': _L0_cond_in['W'], 'L0_cond_b': _L0_cond_in['b'], 'L0_cond_alpha': _L0_cond_in['alpha'], 'L1_cond_Wx': _L1_cond_in['Wx'], 'L1_cond_Wh': _L1_cond_in['Wh'], 'L1_cond_b': _L1_cond_in['b']}

def reference(x, cond_1024, L0_cond_W, L0_cond_b, L0_cond_alpha, L1_cond_Wx, L1_cond_Wh, L1_cond_b):
    import jax
    import jax.numpy as jnp

    def _L0_cond_ref(h_t, z, W, b, alpha):
        import jax, jax.numpy as jnp
        import numpy as np
        LATENT = 512
        D = h_t.shape[-1]
        Wh = W[:, :D]
        Wz = W[:, D:]
        leak = 1.0 - alpha

        def step(h, z_t):
            gate = jax.nn.sigmoid(h @ Wh.T + z_t @ Wz.T + b)
            h_new = jnp.tanh(h * leak + gate * z_t)
            return (h_new, h_new)
        _, hs = jax.lax.scan(step, h_t, jnp.swapaxes(z, 0, 1))
        return jnp.swapaxes(hs, 0, 1)

    def _L1_cond_ref(x, h0, Wx, Wh, b):
        import jax, jax.numpy as jnp
        import numpy as np
        N, T, D, H = (64, 256, 512, 512)
        xw = jnp.einsum('ntd,dh->nth', x, Wx) + b

        def step(prev_h, xw_t):
            next_h = jnp.tanh(xw_t + prev_h @ Wh)
            return (next_h, next_h)
        _, hs = jax.lax.scan(step, h0, jnp.swapaxes(xw, 0, 1))
        return jnp.swapaxes(hs, 0, 1)
    x = x + _L0_cond_ref(cond_1024, x, L0_cond_W, L0_cond_b, L0_cond_alpha)
    x = x + _L1_cond_ref(x, cond_1024, L1_cond_Wx, L1_cond_Wh, L1_cond_b)
    return x

_drawn_inputs = setup_inputs


def setup_inputs(seed=0):
    import zlib

    import numpy as np

    out = dict(_drawn_inputs(seed))
    spreads = {'L0_cond_alpha': (0.10000000149011612, 0.6), 'L1_cond_b': (0.0, 0.1)}
    factors = {'L0_cond_b': 26.719}
    for name, (base, spread) in spreads.items():
        noise = np.random.default_rng([zlib.crc32(name.encode()), seed]).standard_normal(out[name].shape)
        drawn = base * np.exp(spread * noise) if base else spread * noise
        out[name] = jnp.asarray(drawn.astype(out[name].dtype))
    for name, factor in factors.items():
        out[name] = (out[name] * factor).astype(out[name].dtype)
    return out
```

```python
from contextlib import ExitStack

import concourse.bass as bass
from concourse import mybir

F32 = mybir.dt.float32
F32R = mybir.dt.float32r
ALU = mybir.AluOpType
ACT = mybir.ActivationFunctionType

P = 128
CH = 2
RING = 2 * CH
DMA_INC = 16


def cond_recurrences(nc: bass.Bass, x, cond, W0, b0, alpha, Wx, Wh1, b1, out):
    B, T, D = x.shape
    K = D // P
    LOOPS = (T - 2) // RING
    CHUNKS = T // CH
    assert B == P and D % P == 0 and D <= 512 and T % RING == 0

    with ExitStack() as ctx:
        def sb(name, shape, dt=F32):
            return ctx.enter_context(nc.sbuf_tensor(name, shape, dt))

        def bank(name):
            return ctx.enter_context(nc.psum_tensor(name, [P, D], F32))

        def sem(name):
            return ctx.enter_context(nc.semaphore(name))

        ident = sb("ident", [P, P])
        bias0 = sb("bias0", [P, D])
        bias1 = sb("bias1", [P, D])
        leak = sb("leak", [P, D])
        w0_rows = [sb(f"w0_rows_{n}", [P, K, D]) for n in ("wz", "wh0")]
        w1_raw = [sb(f"w1_raw_{n}", [P, K, D]) for n in ("wx", "wh1")]
        wz, wh0, wx, wh1 = [[sb(f"{n}_{part}", [P, K, D], F32R) for part in ("hi", "lo")]
                            for n in ("wz", "wh0", "wx", "wh1")]
        xs = sb("xs", [P, RING, D])
        outs = sb("outs", [P, RING, D])
        h_init = sb("h_init", [P, D])
        pre0 = sb("pre0", [P, D])
        gate = sb("gate", [P, D])
        gated = sb("gated", [P, D])
        leaked = sb("leaked", [P, D])
        arg0 = sb("arg0", [P, D])
        h0 = sb("h0", [P, 2, D])
        x1 = sb("x1", [P, 2, D])
        pre1 = sb("pre1", [P, D])
        h1 = sb("h1", [P, 2, D])
        xT = sb("xT", [P, 2, D])
        x1T = sb("x1T", [P, D])
        xT_hi, xT_lo = sb("xT_hi", [P, D], F32R), sb("xT_lo", [P, D], F32R)
        x1T_hi, x1T_lo = sb("x1T_hi", [P, D], F32R), sb("x1T_lo", [P, D], F32R)
        h0T_hi, h0T_lo = sb("h0T_hi", [P, D], F32R), sb("h0T_lo", [P, D], F32R)
        h1T_hi, h1T_lo = sb("h1T_hi", [P, D], F32R), sb("h1T_lo", [P, D], F32R)
        acc0 = [bank(f"acc0_{i}") for i in range(2)]
        acc1 = [bank(f"acc1_{i}") for i in range(2)]
        turn_x, turn_h0, turn_h1 = bank("turn_x"), bank("turn_h0"), bank("turn_h1")
        turn_w = [bank("turn_w"), *acc1]

        ident_zeroed, ident_ready = sem("ident_zeroed"), sem("ident_ready")
        vec_loaded = sem("vec_loaded")
        leak_ready = sem("leak_ready")
        cond_loaded = sem("cond_loaded")
        w_loaded = {n: sem(f"{n}_loaded") for n in ("wz", "wh0", "wx", "wh1")}
        w0_turned, w0_hi_made, w0_lo_made = sem("w0_turned"), sem("w0_hi_made"), sem("w0_lo_made")
        w1_hi_made, w1_lo_made = sem("w1_hi_made"), sem("w1_lo_made")
        x_loaded = [sem(f"x_loaded_{i}") for i in range(2)]
        stored = [sem(f"stored_{i}") for i in range(2)]
        x_turned, xT_copied = sem("x_turned"), sem("xT_copied")
        xT_hi_made, xT_lo_made = sem("xT_hi_made"), sem("xT_lo_made")
        acc0_done, pre0_made = sem("acc0_done"), sem("pre0_made")
        gate_made, gated_made, leaked_made = sem("gate_made"), sem("gated_made"), sem("leaked_made")
        arg0_made, h0_made = sem("arg0_made"), sem("h0_made")
        h0_turned, h0T_hi_made, h0T_lo_made = sem("h0_turned"), sem("h0T_hi_made"), sem("h0T_lo_made")
        x1T_made, x1T_hi_made, x1T_lo_made = sem("x1T_made"), sem("x1T_hi_made"), sem("x1T_lo_made")
        x1_made = sem("x1_made")
        acc1_done, pre1_made, h1_made = sem("acc1_done"), sem("pre1_made"), sem("h1_made")
        h1_turned, h1T_hi_made, h1T_lo_made = sem("h1_turned"), sem("h1T_hi_made"), sem("h1T_lo_made")
        out_made = sem("out_made")

        def slots(eng, slot, last):
            for s in range(RING + 1):
                slot(0, s)
            with eng.Fori(1, LOOPS) as q:
                for j in range(1, RING + 1):
                    slot(q, j)
            for s in range(LOOPS * RING + 1, last + 1):
                slot(0, s)

        def from_on(first, q, j):
            return not isinstance(q, int) or j >= first

        def before(end, q, j):
            return not isinstance(q, int) or j < end

        block = ctx.enter_context(nc.Block())

        @block.sync
        def _(sp):
            def load_x(c, parity):
                sp.dma_start(xs[:, parity * CH:(parity + 1) * CH, :],
                             x[:, bass.ds(c * CH, CH), :]).then_inc(x_loaded[parity], DMA_INC)

            def store(c, parity):
                sp.dma_start(out[:, bass.ds(c * CH, CH), :],
                             outs[:, parity * CH:(parity + 1) * CH, :]).then_inc(stored[parity], DMA_INC)

            load_x(0, 0)
            sp.dma_start(h_init[:, :], cond).then_inc(cond_loaded, DMA_INC)
            for n, half in (("wz", 1), ("wh0", 0)):
                sp.dma_start(w0_rows[1 - half][:, :, :], W0[:, half * D:(half + 1) * D].rearrange(
                    "(j p) d -> p j d", p=P)).then_inc(w_loaded[n], DMA_INC)
            for dst, src in ((leak, alpha), (bias0, b0), (bias1, b1)):
                sp.dma_start(dst[:, :], src.partition_broadcast(P)).then_inc(vec_loaded, DMA_INC)
            load_x(1, 1)
            for n, dst, src in (("wx", w1_raw[0], Wx), ("wh1", w1_raw[1], Wh1)):
                sp.dma_start(dst[:, :, :], src.rearrange("(k p) n -> p k n", p=P)).then_inc(w_loaded[n], DMA_INC)

            def chunk(q, parity, more):
                c = q * 2 + parity
                if more:
                    sp.wait_ge(x1_made, c * CH + CH)
                    load_x(c + 2, parity)
                sp.wait_ge(out_made, c * CH + CH)
                store(c, parity)

            with sp.Fori(0, CHUNKS // 2 - 1) as q:
                for parity in range(2):
                    chunk(q, parity, True)
            for parity in range(2):
                chunk(CHUNKS // 2 - 1, parity, False)
            for parity in range(2):
                sp.wait_ge(stored[parity], DMA_INC * (CHUNKS // 2))

        @block.tensor
        def _(pe):
            def turn(dst, src):
                for k in range(K):
                    mm = nc.tensor.transpose(dst[:, k * P:(k + 1) * P], src[:, k * P:(k + 1) * P], ident[:, :])
                return mm

            def product(acc, left_hi, left_lo, w, opens, closes, lo_made, lo_count):
                for k in range(K):
                    for n, part in enumerate(w):
                        nc.tensor.matmul(acc[:, :], left_hi[:, k * P:(k + 1) * P], part[:, k, :],
                                         start=opens and k == 0 and n == 0, stop=False)
                pe.wait_ge(lo_made, lo_count)
                for k in range(K):
                    mm = nc.tensor.matmul(acc[:, :], left_lo[:, k * P:(k + 1) * P], w[0][:, k, :],
                                          start=False, stop=closes and k == K - 1)
                return mm

            def turn_step_x(q, j):
                if j % CH == 0:
                    pe.wait_ge(x_loaded[j // CH % 2], (q + j // RING + 1) * DMA_INC)
                if from_on(1, q, j):
                    pe.wait_ge(xT_copied, q * RING + j)
                turn(turn_x, xs[:, j % RING, :]).then_inc(x_turned, 1)

            def input0(q, j):
                pe.wait_ge(xT_hi_made, q * RING + j + 1)
                if from_on(2, q, j):
                    pe.wait_ge(pre0_made, q * RING + j - 1)
                product(acc0[j % 2], xT_hi, xT_lo, wz, True, False, xT_lo_made, q * RING + j + 1)

            def slot(q, j):
                s = q * RING + j
                if before(T, q, j):
                    pe.wait_ge(h0T_hi_made, s + 1)
                    product(acc0[j % 2], h0T_hi, h0T_lo, wh0, False, True,
                            h0T_lo_made, s + 1).then_inc(acc0_done, 1)
                    if before(T - 1, q, j):
                        turn_step_x(q, j + 1)
                if from_on(1, q, j):
                    pe.wait_ge(x1T_hi_made, s)
                    if not from_on(2, q, j):
                        pe.wait_ge(w1_lo_made, K)
                    if from_on(3, q, j):
                        pe.wait_ge(pre1_made, s - 2)
                    product(acc1[(j - 1) % 2], x1T_hi, x1T_lo, wx, True, False, x1T_lo_made, s)
                    pe.wait_ge(h1T_hi_made, s)
                    product(acc1[(j - 1) % 2], h1T_hi, h1T_lo, wh1, False, True,
                            h1T_lo_made, s).then_inc(acc1_done, 1)
                if before(T, q, j):
                    pe.wait_ge(h0_made, s + 1)
                    if from_on(1, q, j):
                        pe.wait_ge(x1T_made, s)
                    turn(turn_h0, h0[:, j % 2, :]).then_inc(h0_turned, 1)
                    if before(T - 1, q, j):
                        input0(q, j + 1)
                if from_on(1, q, j) and before(T, q, j):
                    pe.wait_ge(h1_made, s)
                    turn(turn_h1, h1[:, (j - 1) % 2, :]).then_inc(h1_turned, 1)

            pe.wait_ge(ident_ready, 1)
            turn_step_x(0, 0)
            pe.wait_ge(cond_loaded, DMA_INC)
            turn(turn_h0, h_init).then_inc(h0_turned, 1)
            turn(turn_h1, h_init).then_inc(h1_turned, 1)
            for g in range(2 * K):
                if g % K == 0:
                    pe.wait_ge(w_loaded["wh0" if g else "wz"], DMA_INC)
                if g >= len(turn_w):
                    pe.wait_ge(w0_lo_made, g - len(turn_w) + 1)
                k = g % K
                for jo in range(K):
                    mm = nc.tensor.transpose(turn_w[g % len(turn_w)][:, jo * P:(jo + 1) * P],
                                             w0_rows[g // K][:, jo, k * P:(k + 1) * P], ident[:, :])
                mm.then_inc(w0_turned, 1)
            pe.wait_ge(w0_lo_made, K)
            input0(0, 0)
            pe.wait_ge(w0_lo_made, 2 * K)
            slots(pe, slot, T)

        @block.scalar
        def _(act):
            def copy_xT(q, j):
                act.wait_ge(x_turned, q * RING + j + 1)
                if from_on(2, q, j):
                    act.wait_ge(x1T_made, q * RING + j - 1)
                nc.scalar.activation(xT[:, j % 2, :], turn_x[:, :], ACT.Copy).then_inc(xT_copied, 1)

            def slot(q, j):
                s = q * RING + j
                if before(T, q, j):
                    if before(T - 1, q, j):
                        copy_xT(q, j + 1)
                    act.wait_ge(pre0_made, s + 1)
                    nc.scalar.activation(gate[:, :], pre0[:, :], ACT.Sigmoid).then_inc(gate_made, 1)
                    act.wait_ge(arg0_made, s + 1)
                    nc.scalar.activation(h0[:, j % 2, :], arg0[:, :], ACT.Tanh).then_inc(h0_made, 1)
                    act.wait_ge(h0_turned, s + 2)
                    nc.scalar.activation(h0T_hi[:, :], turn_h0[:, :], ACT.Copy).then_inc(h0T_hi_made, 1)
                if from_on(1, q, j):
                    act.wait_ge(pre1_made, s)
                    if from_on(3, q, j):
                        act.wait_ge(out_made, s - 2)
                    nc.scalar.activation(h1[:, (j - 1) % 2, :], pre1[:, :], ACT.Tanh).then_inc(h1_made, 1)
                if before(T, q, j):
                    act.wait_ge(x1T_made, s + 1)
                    nc.scalar.activation(x1T_hi[:, :], x1T[:, :], ACT.Copy).then_inc(x1T_hi_made, 1)
                if from_on(1, q, j) and before(T, q, j):
                    act.wait_ge(h1_turned, s + 1)
                    nc.scalar.activation(h1T_hi[:, :], turn_h1[:, :], ACT.Copy).then_inc(h1T_hi_made, 1)
                if not from_on(1, q, j):
                    for w, raw, n in ((wx, w1_raw[0], "wx"), (wh1, w1_raw[1], "wh1")):
                        act.wait_ge(w_loaded[n], DMA_INC)
                        for k in range(0, K, 2):
                            nc.scalar.activation(w[0][:, k:k + 2, :], raw[:, k:k + 2, :],
                                                 ACT.Copy).then_inc(w1_hi_made, 1)

            copy_xT(0, 0)
            act.wait_ge(h0_turned, 1)
            nc.scalar.activation(h0T_hi[:, :], turn_h0[:, :], ACT.Copy).then_inc(h0T_hi_made, 1)
            act.wait_ge(h1_turned, 1)
            nc.scalar.activation(h1T_hi[:, :], turn_h1[:, :], ACT.Copy).then_inc(h1T_hi_made, 1)
            for g in range(2 * K):
                act.wait_ge(w0_turned, g + 1)
                nc.scalar.activation((wh0 if g // K else wz)[0][:, g % K, :], turn_w[g % len(turn_w)][:, :],
                                     ACT.Copy).then_inc(w0_hi_made, 1)
            slots(act, slot, T)

        @block.vector
        def _(dve):
            def low_part(lo, whole, hi, done):
                nc.vector.tensor_tensor(lo, whole, hi.bitcast(F32), ALU.subtract).then_inc(done, 1)

            def xT_high(q, j):
                dve.wait_ge(xT_copied, q * RING + j + 1)
                nc.vector.tensor_copy(xT_hi[:, :], xT[:, j % 2, :]).then_inc(xT_hi_made, 1)

            def xT_low(q, j):
                dve.wait_ge(xT_hi_made, q * RING + j + 1)
                low_part(xT_lo[:, :], xT[:, j % 2, :], xT_hi[:, :], xT_lo_made)

            def slot(q, j):
                s = q * RING + j
                if before(T, q, j):
                    more = before(T - 1, q, j)
                    dve.wait_ge(acc0_done, s + 1)
                    nc.vector.tensor_tensor(pre0[:, :], acc0[j % 2][:, :], bias0[:, :],
                                            ALU.add).then_inc(pre0_made, 1)
                    if more:
                        xT_high(q, j + 1)
                    dve.wait_ge(gate_made, s + 1)
                    nc.vector.tensor_tensor(gated[:, :], gate[:, :], xs[:, j % RING, :],
                                            ALU.mult).then_inc(gated_made, 1)
                    dve.wait_ge(gated_made, s + 1)
                    dve.wait_ge(leaked_made, s + 1)
                    nc.vector.tensor_tensor(arg0[:, :], leaked[:, :], gated[:, :],
                                            ALU.add).then_inc(arg0_made, 1)
                    if more:
                        xT_low(q, j + 1)
                if from_on(1, q, j):
                    dve.wait_ge(acc1_done, s)
                    nc.vector.tensor_tensor(pre1[:, :], acc1[(j - 1) % 2][:, :], bias1[:, :],
                                            ALU.add).then_inc(pre1_made, 1)
                if before(T, q, j):
                    dve.wait_ge(h0T_hi_made, s + 2)
                    low_part(h0T_lo[:, :], turn_h0[:, :], h0T_hi[:, :], h0T_lo_made)
                    nc.vector.tensor_tensor(x1T[:, :], turn_h0[:, :], xT[:, j % 2, :],
                                            ALU.add).then_inc(x1T_made, 1)
                    dve.wait_ge(x1T_hi_made, s + 1)
                    low_part(x1T_lo[:, :], x1T[:, :], x1T_hi[:, :], x1T_lo_made)
                if from_on(1, q, j) and before(T, q, j):
                    dve.wait_ge(h1T_hi_made, s + 1)
                    low_part(h1T_lo[:, :], turn_h1[:, :], h1T_hi[:, :], h1T_lo_made)
                if not from_on(1, q, j):
                    n = 0
                    for w, raw in ((wx, w1_raw[0]), (wh1, w1_raw[1])):
                        for k in range(0, K, 2):
                            n += 1
                            dve.wait_ge(w1_hi_made, n)
                            low_part(w[1][:, k:k + 2, :], raw[:, k:k + 2, :], w[0][:, k:k + 2, :], w1_lo_made)

            xT_high(0, 0)
            xT_low(0, 0)
            dve.wait_ge(h0T_hi_made, 1)
            low_part(h0T_lo[:, :], turn_h0[:, :], h0T_hi[:, :], h0T_lo_made)
            dve.wait_ge(h1T_hi_made, 1)
            low_part(h1T_lo[:, :], turn_h1[:, :], h1T_hi[:, :], h1T_lo_made)
            for g in range(2 * K):
                dve.wait_ge(w0_hi_made, g + 1)
                w = wh0 if g // K else wz
                low_part(w[1][:, g % K, :], turn_w[g % len(turn_w)][:, :], w[0][:, g % K, :], w0_lo_made)
            dve.wait_ge(vec_loaded, 3 * DMA_INC)
            nc.vector.tensor_scalar(leak[:, :], leak[:, :], -1.0, 1.0, ALU.mult, ALU.add).then_inc(leak_ready, 1)
            slots(dve, slot, T)

        @block.gpsimd
        def _(pool):
            nc.gpsimd.memset(ident[:, :], 0.0).then_inc(ident_zeroed, 1)
            pool.wait_ge(ident_zeroed, 1)
            nc.gpsimd.affine_select(out=ident[:, :], in_=ident[:, :], compare_op=ALU.not_equal, fill=1.0,
                                    base=0, pattern=[[-1, P]], channel_multiplier=1).then_inc(ident_ready, 1)
            pool.wait_ge(cond_loaded, DMA_INC)
            pool.wait_ge(leak_ready, 1)
            nc.gpsimd.tensor_tensor(leaked[:, :], h_init[:, :], leak[:, :], ALU.mult).then_inc(leaked_made, 1)

            def slot(q, j):
                s = q * RING + j
                if before(T, q, j):
                    pool.wait_ge(h0_made, s + 1)
                    if before(T - 1, q, j):
                        nc.gpsimd.tensor_tensor(leaked[:, :], h0[:, j % 2, :], leak[:, :],
                                                ALU.mult).then_inc(leaked_made, 1)
                    if from_on(2, q, j):
                        pool.wait_ge(out_made, s - 1)
                    nc.gpsimd.tensor_tensor(x1[:, j % 2, :], xs[:, j % RING, :], h0[:, j % 2, :],
                                            ALU.add).then_inc(x1_made, 1)
                if from_on(1, q, j):
                    m = j - 1
                    pool.wait_ge(h1_made, s)
                    pool.wait_ge(x1_made, s)
                    if m % CH == 0 and from_on(2 * CH, q, m):
                        pool.wait_ge(stored[m // CH % 2], (q + m // RING) * DMA_INC)
                    nc.gpsimd.tensor_tensor(outs[:, m % RING, :], x1[:, m % 2, :], h1[:, m % 2, :],
                                            ALU.add).then_inc(out_made, 1)

            slots(pool, slot, T)


_INS = ["x", "cond_1024", "L0_cond_W", "L0_cond_b", "L0_cond_alpha", "L1_cond_Wx", "L1_cond_Wh", "L1_cond_b"]


def kernel(**inputs):
    import numpy as _np
    import concourse.bacc as _bacc
    from concourse import mybir as _mybir
    from concourse.bass_utils import run_bass_kernel_spmd as _run

    nc = _bacc.Bacc("TRN2", target_bir_lowering=False, num_devices=1)
    arrays, args = {}, []
    for name in _INS:
        a = _np.ascontiguousarray(inputs[name])
        arrays[f"in_{name}_dram"] = a
        args.append(nc.dram_tensor(f"in_{name}_dram", a.shape, _mybir.dt.from_np(a.dtype),
                                   kind="ExternalInput").ap())
    args.append(nc.dram_tensor("out_dram", inputs["x"].shape, _mybir.dt.float32, kind="ExternalOutput").ap())
    cond_recurrences(nc, *args)
    r = _run(nc, [arrays], core_ids=[0])
    return r.results[0]["out_dram"]
```

```python
from contextlib import ExitStack

import concourse.bass as bass
from concourse import mybir

F32 = mybir.dt.float32
F32R = mybir.dt.float32r
ALU = mybir.AluOpType
ACT = mybir.ActivationFunctionType

P = 128
QUAD = 32
NQ = P // QUAD
CH = 2
RING = 2 * CH
DMA_INC = 16


def cond_recurrences(nc: bass.Bass, x, cond, W0, b0, alpha, Wx, Wh1, b1, out):
    B, T, D = x.shape
    K = D // P
    LOOPS = (T - 2) // RING
    CHUNKS = T // CH
    assert B == P and D == NQ * P and T % RING == 0

    with ExitStack() as ctx:
        def sb(name, shape, dt=F32):
            return ctx.enter_context(nc.sbuf_tensor(name, shape, dt))

        def bank(name):
            return ctx.enter_context(nc.psum_tensor(name, [P, D], F32))

        def sem(name):
            return ctx.enter_context(nc.semaphore(name))

        ident = sb("ident", [P, P])
        bias0 = sb("bias0", [P, D])
        bias1 = sb("bias1", [P, D])
        leak = sb("leak", [P, D])
        w0_rows = [sb(f"w0_rows_{n}", [P, K, D]) for n in ("wz", "wh0")]
        w1_raw = [sb(f"w1_raw_{n}", [P, K, D]) for n in ("wx", "wh1")]
        wz, wh0, wx, wh1 = [[sb(f"{n}_{part}", [P, K, D], F32R) for part in ("hi", "lo")]
                            for n in ("wz", "wh0", "wx", "wh1")]
        xs = sb("xs", [P, RING, D])
        xq = sb("xq", [P, 2, NQ, CH, P])
        h1q = sb("h1q", [P, D])
        outs = sb("outs", [P, RING, D])
        h_init = sb("h_init", [P, D])
        pre0 = sb("pre0", [P, D])
        gate = sb("gate", [P, D])
        gated = sb("gated", [P, D])
        leaked = sb("leaked", [P, D])
        arg0 = sb("arg0", [P, D])
        h0 = sb("h0", [P, 2, D])
        x1 = sb("x1", [P, 2, D])
        pre1 = sb("pre1", [P, D])
        h1 = sb("h1", [P, 2, D])
        xT = sb("xT", [P, 2, D])
        h1T = sb("h1T", [P, D])
        x1T = sb("x1T", [P, D])
        xT_hi, xT_lo = sb("xT_hi", [P, D], F32R), sb("xT_lo", [P, D], F32R)
        x1T_hi, x1T_lo = sb("x1T_hi", [P, D], F32R), sb("x1T_lo", [P, D], F32R)
        h0T_hi, h0T_lo = sb("h0T_hi", [P, D], F32R), sb("h0T_lo", [P, D], F32R)
        h1T_hi, h1T_lo = sb("h1T_hi", [P, D], F32R), sb("h1T_lo", [P, D], F32R)
        acc0 = [bank(f"acc0_{i}") for i in range(2)]
        acc1 = [bank(f"acc1_{i}") for i in range(2)]
        turn_h0 = bank("turn_h0")
        turn_w = [bank("turn_w"), *acc1]

        ident_zeroed, ident_ready = sem("ident_zeroed"), sem("ident_ready")
        vec_loaded = sem("vec_loaded")
        leak_ready = sem("leak_ready")
        cond_loaded = sem("cond_loaded")
        w_loaded = {n: sem(f"{n}_loaded") for n in ("wz", "wh0", "wx", "wh1")}
        w0_turned, w0_hi_made, w0_lo_made = sem("w0_turned"), sem("w0_hi_made"), sem("w0_lo_made")
        w1_hi_made, w1_lo_made = sem("w1_hi_made"), sem("w1_lo_made")
        x_loaded = [sem(f"x_loaded_{i}") for i in range(2)]
        xq_loaded = [sem(f"xq_loaded_{i}") for i in range(2)]
        stored = [sem(f"stored_{i}") for i in range(2)]
        x_turned = sem("x_turned")
        xT_hi_made, xT_lo_made = sem("xT_hi_made"), sem("xT_lo_made")
        acc0_done, pre0_made = sem("acc0_done"), sem("pre0_made")
        gate_made, gated_made, leaked_made = sem("gate_made"), sem("gated_made"), sem("leaked_made")
        arg0_made, h0_made = sem("arg0_made"), sem("h0_made")
        h0_turned, h0T_hi_made, h0T_lo_made = sem("h0_turned"), sem("h0T_hi_made"), sem("h0T_lo_made")
        x1T_made, x1T_hi_made, x1T_lo_made = sem("x1T_made"), sem("x1T_hi_made"), sem("x1T_lo_made")
        x1_made = sem("x1_made")
        acc1_done, pre1_made, h1_made = sem("acc1_done"), sem("pre1_made"), sem("h1_made")
        h1_spread, h1_turned, h1T_hi_made, h1T_lo_made = sem("h1_spread"), sem("h1_turned"), sem("h1T_hi_made"), sem("h1T_lo_made")
        out_made = sem("out_made")

        def slots(eng, slot, last):
            for s in range(RING + 1):
                slot(0, s)
            with eng.Fori(1, LOOPS) as q:
                for j in range(1, RING + 1):
                    slot(q, j)
            for s in range(LOOPS * RING + 1, last + 1):
                slot(0, s)

        def from_on(first, q, j):
            return not isinstance(q, int) or j >= first

        def before(end, q, j):
            return not isinstance(q, int) or j < end

        def in_quadrant(rows, q):
            return rows[..., q * P:(q + 1) * P]

        block = ctx.enter_context(nc.Block())

        @block.sync
        def _(sp):
            def load_x(first, parity):
                sp.dma_start(xs[:, parity * CH:(parity + 1) * CH, :],
                             x[:, bass.ds(first, CH), :]).then_inc(x_loaded[parity], DMA_INC)

            def load_xq(first, parity):
                for q in range(NQ):
                    sp.dma_start(xq[q * QUAD:(q + 1) * QUAD, parity].rearrange("b r t f -> b (r t) f"),
                                 in_quadrant(x[:, bass.ds(first, CH), :], q)).then_inc(xq_loaded[parity], DMA_INC)

            def store(first, parity):
                sp.dma_start(out[:, bass.ds(first, CH), :],
                             outs[:, parity * CH:(parity + 1) * CH, :]).then_inc(stored[parity], DMA_INC)

            def spread_h1(half):
                for q in range(NQ):
                    sp.dma_start(h1q[q * QUAD:(q + 1) * QUAD, :].rearrange("b (r f) -> b r f", r=NQ),
                                 in_quadrant(h1[:, half, :], q)).then_inc(h1_spread, DMA_INC)

            def held(step):
                return step if isinstance(step, int) else sp.snap(step)

            def slot(q, j):
                s = held(q * RING + j)
                after_s = held(q * RING + j + 1)
                load = j % CH == CH - 1 and before(T - 2 * CH, q, j)
                stores = from_on(1, q, j) and (j - 1) % CH == CH - 1
                if load:
                    load_from = held(q * RING + j + 1 + CH)
                if stores:
                    store_from = held(q * RING + j - CH)
                if from_on(1, q, j) and before(T, q, j):
                    sp.wait_ge(h1_made, s)
                    spread_h1((j - 1) % 2)
                if load:
                    sp.wait_ge(x1_made, after_s)
                    load_x(load_from, j // CH % 2)
                    load_xq(load_from, j // CH % 2)
                if stores:
                    sp.wait_ge(out_made, s)
                    store(store_from, (j - 1) // CH % 2)

            load_xq(0, 0)
            sp.dma_start(h_init[:, :], cond).then_inc(cond_loaded, DMA_INC)
            for n, half in (("wz", 1), ("wh0", 0)):
                sp.dma_start(w0_rows[1 - half][:, :, :], W0[:, half * D:(half + 1) * D].rearrange(
                    "(j p) d -> p j d", p=P)).then_inc(w_loaded[n], DMA_INC)
            load_x(0, 0)
            for dst, src in ((leak, alpha), (bias0, b0), (bias1, b1)):
                sp.dma_start(dst[:, :], src.partition_broadcast(P)).then_inc(vec_loaded, DMA_INC)
            for n, dst, src in (("wx", w1_raw[0], Wx), ("wh1", w1_raw[1], Wh1)):
                sp.dma_start(dst[:, :, :], src.rearrange("(m c) n -> m c n", c=K)).then_inc(w_loaded[n], DMA_INC)
            load_xq(CH, 1)
            load_x(CH, 1)
            slots(sp, slot, T)
            for parity in range(2):
                sp.wait_ge(stored[parity], DMA_INC * (CHUNKS // 2))

        @block.tensor
        def _(pe):
            def turn(dst, src):
                for c in range(K):
                    mm = nc.tensor.transpose(dst[:, c * P:(c + 1) * P], src[:, c:D:K], ident[:, :])
                return mm

            def product(acc, left_hi, left_lo, w, opens, closes, lo_made, lo_count):
                for k in range(K):
                    for n, part in enumerate(w):
                        nc.tensor.matmul(acc[:, :], left_hi[:, k * P:(k + 1) * P], part[:, k, :],
                                         start=opens and k == 0 and n == 0, stop=False)
                pe.wait_ge(lo_made, lo_count)
                for k in range(K):
                    mm = nc.tensor.matmul(acc[:, :], left_lo[:, k * P:(k + 1) * P], w[0][:, k, :],
                                          start=False, stop=closes and k == K - 1)
                return mm

            def input0(q, j):
                pe.wait_ge(xT_hi_made, q * RING + j + 1)
                if from_on(2, q, j):
                    pe.wait_ge(pre0_made, q * RING + j - 1)
                product(acc0[j % 2], xT_hi, xT_lo, wz, True, False, xT_lo_made, q * RING + j + 1)

            def slot(q, j):
                s = q * RING + j
                if before(T, q, j):
                    pe.wait_ge(h0T_hi_made, s + 1)
                    product(acc0[j % 2], h0T_hi, h0T_lo, wh0, False, True,
                            h0T_lo_made, s + 1).then_inc(acc0_done, 1)
                if from_on(1, q, j):
                    pe.wait_ge(x1T_hi_made, s)
                    if not from_on(2, q, j):
                        pe.wait_ge(w1_lo_made, K)
                    if from_on(3, q, j):
                        pe.wait_ge(pre1_made, s - 2)
                    product(acc1[(j - 1) % 2], x1T_hi, x1T_lo, wx, True, False, x1T_lo_made, s)
                    pe.wait_ge(h1T_hi_made, s)
                    product(acc1[(j - 1) % 2], h1T_hi, h1T_lo, wh1, False, True,
                            h1T_lo_made, s).then_inc(acc1_done, 1)
                if before(T, q, j):
                    pe.wait_ge(h0_made, s + 1)
                    if from_on(1, q, j):
                        pe.wait_ge(x1T_made, s)
                    turn(turn_h0, h0[:, j % 2, :]).then_inc(h0_turned, 1)
                    if before(T - 1, q, j):
                        input0(q, j + 1)

            pe.wait_ge(ident_ready, 1)
            pe.wait_ge(cond_loaded, DMA_INC)
            turn(turn_h0, h_init).then_inc(h0_turned, 1)
            for g in range(2 * K):
                if g % K == 0:
                    pe.wait_ge(w_loaded["wh0" if g else "wz"], DMA_INC)
                if g >= len(turn_w):
                    pe.wait_ge(w0_lo_made, g - len(turn_w) + 1)
                for jo in range(K):
                    mm = nc.tensor.transpose(turn_w[g % len(turn_w)][:, jo * P:(jo + 1) * P],
                                             w0_rows[g // K][:, jo, g % K:D:K], ident[:, :])
                mm.then_inc(w0_turned, 1)
            pe.wait_ge(w0_lo_made, K)
            input0(0, 0)
            pe.wait_ge(w0_lo_made, 2 * K)
            slots(pe, slot, T)

        @block.scalar
        def _(act):
            def slot(q, j):
                s = q * RING + j
                if before(T, q, j):
                    act.wait_ge(pre0_made, s + 1)
                    nc.scalar.activation(gate[:, :], pre0[:, :], ACT.Sigmoid).then_inc(gate_made, 1)
                    act.wait_ge(arg0_made, s + 1)
                    if from_on(2, q, j):
                        act.wait_ge(x1_made, s - 1)
                    nc.scalar.activation(h0[:, j % 2, :], arg0[:, :], ACT.Tanh).then_inc(h0_made, 1)
                    act.wait_ge(h0_turned, s + 2)
                    nc.scalar.activation(h0T_hi[:, :], turn_h0[:, :], ACT.Copy).then_inc(h0T_hi_made, 1)
                if from_on(1, q, j):
                    act.wait_ge(pre1_made, s)
                    if from_on(3, q, j):
                        act.wait_ge(out_made, s - 2)
                        act.wait_ge(h1_spread, (s - 2) * NQ * DMA_INC)
                    nc.scalar.activation(h1[:, (j - 1) % 2, :], pre1[:, :], ACT.Tanh).then_inc(h1_made, 1)
                if not from_on(1, q, j):
                    for w, raw, n in ((wx, w1_raw[0], "wx"), (wh1, w1_raw[1], "wh1")):
                        act.wait_ge(w_loaded[n], DMA_INC)
                        for k in range(0, K, 2):
                            nc.scalar.activation(w[0][:, k:k + 2, :], raw[:, k:k + 2, :],
                                                 ACT.Copy).then_inc(w1_hi_made, 1)

            act.wait_ge(h0_turned, 1)
            nc.scalar.activation(h0T_hi[:, :], turn_h0[:, :], ACT.Copy).then_inc(h0T_hi_made, 1)
            nc.scalar.activation(h1T_hi[:, :], turn_h0[:, :], ACT.Copy).then_inc(h1T_hi_made, 1)
            for g in range(2 * K):
                act.wait_ge(w0_turned, g + 1)
                nc.scalar.activation((wh0 if g // K else wz)[0][:, g % K, :], turn_w[g % len(turn_w)][:, :],
                                     ACT.Copy).then_inc(w0_hi_made, 1)
            slots(act, slot, T)

        @block.vector
        def _(dve):
            def low_part(lo, whole, hi, done):
                nc.vector.tensor_tensor(lo, whole, hi.bitcast(F32), ALU.subtract).then_inc(done, 1)

            def turn_quadrants(dst, src, done):
                nc.vector.transpose(dst.rearrange("p (c b r) -> p r c b", c=K, r=NQ),
                                    src.rearrange("p r (f c) -> p r c f", c=K)).then_inc(done, 1)

            def split(hi, lo, whole, hi_made, lo_made, n):
                nc.vector.tensor_copy(hi[:, :], whole).then_inc(hi_made, 1)
                dve.wait_ge(hi_made, n)
                low_part(lo[:, :], whole, hi[:, :], lo_made)

            def turn_x(q, j):
                if j % CH == 0:
                    dve.wait_ge(xq_loaded[j // CH % 2], (q + j // RING + 1) * NQ * DMA_INC)
                turn_quadrants(xT[:, j % 2, :], xq[:, j // CH % 2, :, j % CH, :], x_turned)

            def split_x(q, j):
                dve.wait_ge(x_turned, q * RING + j + 1)
                split(xT_hi, xT_lo, xT[:, j % 2, :], xT_hi_made, xT_lo_made, q * RING + j + 1)

            def turn_h1(n):
                dve.wait_ge(h1_spread, n * NQ * DMA_INC)
                turn_quadrants(h1T[:, :], h1q[:, :].rearrange("p (r f) -> p r f", r=NQ), h1_turned)
                dve.wait_ge(h1_turned, n)
                nc.vector.tensor_copy(h1T_hi[:, :], h1T[:, :]).then_inc(h1T_hi_made, 1)

            def low_h1(n):
                dve.wait_ge(h1T_hi_made, n + 1)
                low_part(h1T_lo[:, :], h1T[:, :], h1T_hi[:, :], h1T_lo_made)

            def slot(q, j):
                s = q * RING + j
                if before(T, q, j):
                    dve.wait_ge(acc0_done, s + 1)
                    nc.vector.tensor_tensor(pre0[:, :], acc0[j % 2][:, :], bias0[:, :],
                                            ALU.add).then_inc(pre0_made, 1)
                if from_on(2, q, j):
                    turn_h1(s - 1)
                if before(T, q, j):
                    dve.wait_ge(gate_made, s + 1)
                    if j % CH == 0:
                        dve.wait_ge(x_loaded[j // CH % 2], (q + j // RING + 1) * DMA_INC)
                    nc.vector.tensor_tensor(gated[:, :], gate[:, :], xs[:, j % RING, :],
                                            ALU.mult).then_inc(gated_made, 1)
                    dve.wait_ge(gated_made, s + 1)
                    dve.wait_ge(leaked_made, s + 1)
                    nc.vector.tensor_tensor(arg0[:, :], leaked[:, :], gated[:, :],
                                            ALU.add).then_inc(arg0_made, 1)
                if from_on(2, q, j):
                    low_h1(s - 1)
                if before(T - 1, q, j):
                    split_x(q, j + 1)
                if from_on(1, q, j):
                    dve.wait_ge(acc1_done, s)
                    nc.vector.tensor_tensor(pre1[:, :], acc1[(j - 1) % 2][:, :], bias1[:, :],
                                            ALU.add).then_inc(pre1_made, 1)
                if before(T, q, j):
                    dve.wait_ge(h0T_hi_made, s + 2)
                    low_part(h0T_lo[:, :], turn_h0[:, :], h0T_hi[:, :], h0T_lo_made)
                    nc.vector.tensor_tensor(x1T[:, :], turn_h0[:, :], xT[:, j % 2, :],
                                            ALU.add).then_inc(x1T_made, 1)
                    dve.wait_ge(x1T_made, s + 1)
                    split(x1T_hi, x1T_lo, x1T[:, :], x1T_hi_made, x1T_lo_made, s + 1)
                if before(T - 2, q, j):
                    turn_x(q, j + 2)
                if not from_on(1, q, j):
                    n = 0
                    for w, raw in ((wx, w1_raw[0]), (wh1, w1_raw[1])):
                        for k in range(0, K, 2):
                            n += 1
                            dve.wait_ge(w1_hi_made, n)
                            low_part(w[1][:, k:k + 2, :], raw[:, k:k + 2, :], w[0][:, k:k + 2, :], w1_lo_made)

            turn_x(0, 0)
            turn_x(0, 1)
            split_x(0, 0)
            dve.wait_ge(h1T_hi_made, 1)
            low_part(h0T_lo[:, :], turn_h0[:, :], h0T_hi[:, :], h0T_lo_made)
            low_part(h1T_lo[:, :], turn_h0[:, :], h1T_hi[:, :], h1T_lo_made)
            for g in range(2 * K):
                dve.wait_ge(w0_hi_made, g + 1)
                w = wh0 if g // K else wz
                low_part(w[1][:, g % K, :], turn_w[g % len(turn_w)][:, :], w[0][:, g % K, :], w0_lo_made)
            dve.wait_ge(vec_loaded, 3 * DMA_INC)
            nc.vector.tensor_scalar(leak[:, :], leak[:, :], -1.0, 1.0, ALU.mult, ALU.add).then_inc(leak_ready, 1)
            slots(dve, slot, T)

        @block.gpsimd
        def _(pool):
            nc.gpsimd.memset(ident[:, :], 0.0).then_inc(ident_zeroed, 1)
            pool.wait_ge(ident_zeroed, 1)
            nc.gpsimd.affine_select(out=ident[:, :], in_=ident[:, :], compare_op=ALU.not_equal, fill=1.0,
                                    base=0, pattern=[[-1, P]], channel_multiplier=1).then_inc(ident_ready, 1)
            pool.wait_ge(cond_loaded, DMA_INC)
            pool.wait_ge(leak_ready, 1)
            nc.gpsimd.tensor_tensor(leaked[:, :], h_init[:, :], leak[:, :], ALU.mult).then_inc(leaked_made, 1)

            def slot(q, j):
                s = q * RING + j
                if before(T, q, j):
                    pool.wait_ge(h0_made, s + 1)
                    if j % CH == 0:
                        pool.wait_ge(x_loaded[j // CH % 2], (q + j // RING + 1) * DMA_INC)
                    if from_on(2, q, j):
                        pool.wait_ge(out_made, s - 1)
                    nc.gpsimd.tensor_tensor(x1[:, j % 2, :], xs[:, j % RING, :], h0[:, j % 2, :],
                                            ALU.add).then_inc(x1_made, 1)
                    if before(T - 1, q, j):
                        nc.gpsimd.tensor_tensor(leaked[:, :], h0[:, j % 2, :], leak[:, :],
                                                ALU.mult).then_inc(leaked_made, 1)
                if from_on(1, q, j):
                    m = j - 1
                    pool.wait_ge(h1_made, s)
                    pool.wait_ge(x1_made, s)
                    if m % CH == 0 and from_on(2 * CH, q, m):
                        pool.wait_ge(stored[m // CH % 2], (q + m // RING) * DMA_INC)
                    nc.gpsimd.tensor_tensor(outs[:, m % RING, :], x1[:, m % 2, :], h1[:, m % 2, :],
                                            ALU.add).then_inc(out_made, 1)

            slots(pool, slot, T)


_INS = ["x", "cond_1024", "L0_cond_W", "L0_cond_b", "L0_cond_alpha", "L1_cond_Wx", "L1_cond_Wh", "L1_cond_b"]


def kernel(**inputs):
    import numpy as _np
    import concourse.bacc as _bacc
    from concourse import mybir as _mybir
    from concourse.bass_utils import run_bass_kernel_spmd as _run

    nc = _bacc.Bacc("TRN2", target_bir_lowering=False, num_devices=1)
    arrays, args = {}, []
    for name in _INS:
        a = _np.ascontiguousarray(inputs[name])
        arrays[f"in_{name}_dram"] = a
        args.append(nc.dram_tensor(f"in_{name}_dram", a.shape, _mybir.dt.from_np(a.dtype),
                                   kind="ExternalInput").ap())
    args.append(nc.dram_tensor("out_dram", inputs["x"].shape, _mybir.dt.float32, kind="ExternalOutput").ap())
    cond_recurrences(nc, *args)
    r = _run(nc, [arrays], core_ids=[0])
    return r.results[0]["out_dram"]
```

```python
from contextlib import ExitStack

import concourse.bass as bass
from concourse import mybir

F32 = mybir.dt.float32
F32R = mybir.dt.float32r
ALU = mybir.AluOpType
ACT = mybir.ActivationFunctionType

P = 128
QUAD = 32
NQ = P // QUAD
CH = 2
RING = 2 * CH
DMA_INC = 16


def cond_recurrences(nc: bass.Bass, x, cond, W0, b0, alpha, Wx, Wh1, b1, out):
    B, T, D = x.shape
    K = D // P
    LOOPS = (T - 2) // RING
    CHUNKS = T // CH
    assert B == P and D == NQ * P and T % RING == 0

    with ExitStack() as ctx:
        def sb(name, shape, dt=F32):
            return ctx.enter_context(nc.sbuf_tensor(name, shape, dt))

        def bank(name):
            return ctx.enter_context(nc.psum_tensor(name, [P, D], F32))

        def sem(name):
            return ctx.enter_context(nc.semaphore(name))

        ident = sb("ident", [P, P])
        bias0 = sb("bias0", [P, D])
        bias1 = sb("bias1", [P, D])
        leak = sb("leak", [P, D])
        w0_rows = [sb(f"w0_rows_{n}", [P, K, D]) for n in ("wz", "wh0")]
        w1_raw = [sb(f"w1_raw_{n}", [P, K, D]) for n in ("wx", "wh1")]
        wz, wh0, wx, wh1 = [[sb(f"{n}_{part}", [P, K, D], F32R) for part in ("hi", "lo")]
                            for n in ("wz", "wh0", "wx", "wh1")]
        xs = sb("xs", [P, RING, D])
        xq = sb("xq", [P, 2, NQ, CH, P])
        h1q = sb("h1q", [P, D])
        outs = sb("outs", [P, RING, D])
        h_init = sb("h_init", [P, D])
        pre0 = sb("pre0", [P, D])
        gate = sb("gate", [P, D])
        gated = sb("gated", [P, D])
        leaked = sb("leaked", [P, D])
        arg0 = sb("arg0", [P, D])
        h0 = sb("h0", [P, 2, D])
        x1 = sb("x1", [P, 2, D])
        pre1 = sb("pre1", [P, D])
        h1 = sb("h1", [P, 2, D])
        xT = sb("xT", [P, 2, D])
        h1T = sb("h1T", [P, D])
        x1T = sb("x1T", [P, D])
        xT_hi, xT_lo = sb("xT_hi", [P, D], F32R), sb("xT_lo", [P, D], F32R)
        x1T_hi, x1T_lo = sb("x1T_hi", [P, D], F32R), sb("x1T_lo", [P, D], F32R)
        h0T_hi, h0T_lo = sb("h0T_hi", [P, D], F32R), sb("h0T_lo", [P, D], F32R)
        h1T_hi, h1T_lo = sb("h1T_hi", [P, D], F32R), sb("h1T_lo", [P, D], F32R)
        acc0 = [bank(f"acc0_{i}") for i in range(2)]
        acc1 = [bank(f"acc1_{i}") for i in range(2)]
        turn_h0 = bank("turn_h0")
        turn_w = [bank("turn_w"), *acc1]

        ident_zeroed, ident_ready = sem("ident_zeroed"), sem("ident_ready")
        vec_loaded = sem("vec_loaded")
        leak_ready = sem("leak_ready")
        cond_loaded = sem("cond_loaded")
        w_loaded = {n: sem(f"{n}_loaded") for n in ("wz", "wh0", "wx", "wh1")}
        w0_turned, w0_hi_made, w0_lo_made = sem("w0_turned"), sem("w0_hi_made"), sem("w0_lo_made")
        w1_hi_made, w1_lo_made = sem("w1_hi_made"), sem("w1_lo_made")
        x_loaded = [sem(f"x_loaded_{i}") for i in range(2)]
        xq_loaded = [sem(f"xq_loaded_{i}") for i in range(2)]
        stored = [sem(f"stored_{i}") for i in range(2)]
        x_turned = sem("x_turned")
        table_loaded = sem("table_loaded")
        first_input_done = sem("first_input_done")
        xT_hi_made, xT_lo_made = sem("xT_hi_made"), sem("xT_lo_made")
        acc0_done, pre0_made = sem("acc0_done"), sem("pre0_made")
        gate_made, gated_made, leaked_made = sem("gate_made"), sem("gated_made"), sem("leaked_made")
        arg0_made, h0_made = sem("arg0_made"), sem("h0_made")
        h0_turned = sem("h0_turned")
        h0T_hi_made, h0T_lo_made = sem("h0T_hi_made"), sem("h0T_lo_made")
        x1T_made, x1T_hi_made, x1T_lo_made = sem("x1T_made"), sem("x1T_hi_made"), sem("x1T_lo_made")
        x1_made = sem("x1_made")
        acc1_done, pre1_made, h1_made = sem("acc1_done"), sem("pre1_made"), sem("h1_made")
        h1_spread, h1_turned = sem("h1_spread"), sem("h1_turned")
        h1T_hi_made, h1T_lo_made = sem("h1T_hi_made"), sem("h1T_lo_made")
        out_made, last_out_made = sem("out_made"), sem("last_out_made")

        def slots(eng, slot, last):
            for s in range(RING + 1):
                slot(0, s)
            with eng.Fori(1, LOOPS) as q:
                for j in range(1, RING + 1):
                    slot(q, j)
            for s in range(LOOPS * RING + 1, last + 1):
                slot(0, s)

        def from_on(first, q, j):
            return not isinstance(q, int) or j >= first

        def before(end, q, j):
            return not isinstance(q, int) or j < end

        def in_quadrant(rows, q):
            return rows[..., q * P:(q + 1) * P]

        block = ctx.enter_context(nc.Block())

        @block.sync
        def _(sp):
            def load_w0(n, half):
                sp.dma_start(w0_rows[1 - half][:, :, :], W0[:, half * D:(half + 1) * D].rearrange(
                    "(j p) d -> p j d", p=P)).then_inc(w_loaded[n], DMA_INC)

            def load_x(first, parity):
                sp.dma_start(xs[:, parity * CH:(parity + 1) * CH, :],
                             x[:, bass.ds(first, CH), :]).then_inc(x_loaded[parity], DMA_INC)

            def load_xq(first, parity):
                for q in range(NQ):
                    sp.dma_start(xq[q * QUAD:(q + 1) * QUAD, parity].rearrange("b r t f -> b (r t) f"),
                                 in_quadrant(x[:, bass.ds(first, CH), :], q)).then_inc(xq_loaded[parity], DMA_INC)

            def store(first, parity):
                sp.dma_start(out[:, bass.ds(first, CH), :],
                             outs[:, parity * CH:(parity + 1) * CH, :]).then_inc(stored[parity], DMA_INC)

            def store_step(step):
                sp.dma_start(out[:, step:step + 1, :],
                             outs[:, step % RING:step % RING + 1, :]).then_inc(stored[1], DMA_INC)

            def spread_h1(half):
                for q in range(NQ):
                    sp.dma_start(h1q[q * QUAD:(q + 1) * QUAD, :].rearrange("b (r f) -> b r f", r=NQ),
                                 in_quadrant(h1[:, half, :], q)).then_inc(h1_spread, DMA_INC)

            def held(step):
                return step if isinstance(step, int) else sp.snap(step)

            def slot(q, j):
                s = held(q * RING + j)
                after_s = held(q * RING + j + 1)
                load = j % CH == CH - 1 and before(T - 2 * CH, q, j)
                stores = from_on(1, q, j) and before(T - CH + 1, q, j) and (j - 1) % CH == CH - 1
                if load:
                    load_from = held(q * RING + j + 1 + CH)
                if stores:
                    store_from = held(q * RING + j - CH)
                if load:
                    sp.wait_ge(x1_made, after_s)
                    load_x(load_from, j // CH % 2)
                    load_xq(load_from, j // CH % 2)
                if from_on(1, q, j) and before(T - 1, q, j):
                    sp.wait_ge(h1_made, s)
                    spread_h1((j - 1) % 2)
                if stores:
                    sp.wait_ge(out_made, s)
                    store(store_from, (j - 1) // CH % 2)
                if not before(T - CH + 1, q, j):
                    if before(T, q, j):
                        sp.wait_ge(out_made, s)
                    else:
                        sp.wait_ge(last_out_made, 1)
                    store_step(s - 1)

            load_w0("wz", 1)
            load_xq(0, 0)
            sp.dma_start(h_init[:, :], cond).then_inc(cond_loaded, DMA_INC)
            load_w0("wh0", 0)
            load_x(0, 0)
            for dst, src in ((leak, alpha), (bias0, b0), (bias1, b1)):
                sp.dma_start(dst[:, :], src.partition_broadcast(P)).then_inc(vec_loaded, DMA_INC)
            for n, dst, src in (("wx", w1_raw[0], Wx), ("wh1", w1_raw[1], Wh1)):
                sp.dma_start(dst[:, :, :], src.rearrange("(m c) n -> m c n", c=K)).then_inc(w_loaded[n], DMA_INC)
            load_xq(CH, 1)
            load_x(CH, 1)
            slots(sp, slot, T)
            sp.wait_ge(stored[0], DMA_INC * (CHUNKS // 2))
            sp.wait_ge(stored[1], DMA_INC * (CHUNKS // 2 - 1 + CH))

        @block.tensor
        def _(pe):
            def turn(dst, src):
                for c in range(K):
                    mm = nc.tensor.transpose(dst[:, c * P:(c + 1) * P], src[:, c:D:K], ident[:, :])
                return mm

            def product(acc, left_hi, left_lo, w, opens, closes, lo_made, lo_count):
                for k in range(K):
                    for n, part in enumerate(w):
                        nc.tensor.matmul(acc[:, :], left_hi[:, k * P:(k + 1) * P], part[:, k, :],
                                         start=opens and k == 0 and n == 0, stop=False)
                pe.wait_ge(lo_made, lo_count)
                for k in range(K):
                    mm = nc.tensor.matmul(acc[:, :], left_lo[:, k * P:(k + 1) * P], w[0][:, k, :],
                                          start=False, stop=closes and k == K - 1)
                return mm

            def input0(q, j):
                pe.wait_ge(xT_hi_made, q * RING + j + 1)
                if from_on(2, q, j):
                    pe.wait_ge(pre0_made, q * RING + j - 1)
                return product(acc0[j % 2], xT_hi, xT_lo, wz, True, False, xT_lo_made, q * RING + j + 1)

            def slot(q, j):
                s = q * RING + j
                if before(T, q, j):
                    pe.wait_ge(h0T_hi_made, s + 1)
                    product(acc0[j % 2], h0T_hi, h0T_lo, wh0, False, True,
                            h0T_lo_made, s + 1).then_inc(acc0_done, 1)
                if from_on(1, q, j):
                    pe.wait_ge(x1T_hi_made, s)
                    if not from_on(2, q, j):
                        pe.wait_ge(w1_lo_made, K // 2)
                    if from_on(3, q, j):
                        pe.wait_ge(pre1_made, s - 2)
                    product(acc1[(j - 1) % 2], x1T_hi, x1T_lo, wx, True, False, x1T_lo_made, s)
                if before(T, q, j):
                    if before(T - 1, q, j):
                        input0(q, j + 1)
                    pe.wait_ge(h0_made, s + 1)
                    if from_on(1, q, j):
                        pe.wait_ge(x1T_made, s)
                    turn(turn_h0, h0[:, j % 2, :]).then_inc(h0_turned, 1)
                if not before(T, q, j):
                    pe.wait_ge(h1_made, s - 1)
                    pe.wait_ge(x1T_made, s)
                    turn(turn_h0, h1[:, j % 2, :]).then_inc(h1_turned, 1)
                if from_on(1, q, j):
                    if not from_on(2, q, j):
                        pe.wait_ge(w1_lo_made, K)
                    pe.wait_ge(h1T_hi_made, s)
                    product(acc1[(j - 1) % 2], h1T_hi, h1T_lo, wh1, False, True,
                            h1T_lo_made, s).then_inc(acc1_done, 1)

            pe.wait_ge(ident_ready, 1)
            for g in range(2 * K):
                if g == K:
                    pe.wait_ge(cond_loaded, DMA_INC)
                    turn(turn_h0, h_init).then_inc(h0_turned, 1)
                if g % K == 0:
                    pe.wait_ge(w_loaded["wh0" if g else "wz"], DMA_INC)
                if g == 2 * K - 1:
                    pe.wait_ge(w0_lo_made, K)
                    input0(0, 0).then_inc(first_input_done, 1)
                if g >= len(turn_w):
                    pe.wait_ge(w0_lo_made, g - len(turn_w) + 1)
                for jo in range(K):
                    mm = nc.tensor.transpose(turn_w[g % len(turn_w)][:, jo * P:(jo + 1) * P],
                                             w0_rows[g // K][:, jo, g % K:D:K], ident[:, :])
                mm.then_inc(w0_turned, 1)
            pe.wait_ge(w0_lo_made, 2 * K)
            slots(pe, slot, T)

        @block.scalar
        def _(act):
            def high_part(hi, whole, done):
                nc.scalar.activation(hi, whole, ACT.Copy).then_inc(done, 1)

            def high_x(q, j):
                act.wait_ge(x_turned, q * RING + j + 1)
                high_part(xT_hi[:, :], xT[:, j % 2, :], xT_hi_made)

            def high_w1(w, raw, n):
                act.wait_ge(w_loaded[n], DMA_INC)
                for k in range(0, K, 2):
                    high_part(w[0][:, k:k + 2, :], raw[:, k:k + 2, :], w1_hi_made)

            def slot(q, j):
                s = q * RING + j
                if before(T, q, j):
                    act.wait_ge(pre0_made, s + 1)
                    nc.scalar.activation(gate[:, :], pre0[:, :], ACT.Sigmoid).then_inc(gate_made, 1)
                    act.wait_ge(arg0_made, s + 1)
                    if from_on(2, q, j):
                        act.wait_ge(x1_made, s - 1)
                    nc.scalar.activation(h0[:, j % 2, :], arg0[:, :], ACT.Tanh).then_inc(h0_made, 1)
                if from_on(2, q, j):
                    act.wait_ge(h1_turned, s - 1)
                    high_part(h1T_hi[:, :], h1T[:, :] if before(T, q, j) else turn_h0[:, :], h1T_hi_made)
                if before(T, q, j):
                    act.wait_ge(h0_turned, s + 2)
                    high_part(h0T_hi[:, :], turn_h0[:, :], h0T_hi_made)
                    act.wait_ge(x1T_made, s + 1)
                    high_part(x1T_hi[:, :], x1T[:, :], x1T_hi_made)
                if not from_on(1, q, j):
                    high_w1(wh1, w1_raw[1], "wh1")
                if from_on(1, q, j):
                    act.wait_ge(pre1_made, s)
                    if from_on(3, q, j):
                        act.wait_ge(out_made, s - 2)
                        act.wait_ge(h1_spread, (s - 2) * NQ * DMA_INC)
                    nc.scalar.activation(h1[:, (j - 1) % 2, :], pre1[:, :], ACT.Tanh).then_inc(h1_made, 1)
                if before(T - 2, q, j):
                    high_x(q, j + 2)

            act.wait_ge(ident_ready, 1)
            nc.scalar.activation(gate[:, 0:1], ident[:, 0:1], ACT.Sigmoid).then_inc(table_loaded, 1)

            def high_w0(g):
                act.wait_ge(w0_turned, g + 1)
                high_part((wh0 if g // K else wz)[0][:, g % K, :], turn_w[g % len(turn_w)][:, :], w0_hi_made)

            for g in range(K):
                high_w0(g)
            high_x(0, 0)
            act.wait_ge(h0_turned, 1)
            high_part(h0T_hi[:, :], turn_h0[:, :], h0T_hi_made)
            high_part(h1T_hi[:, :], turn_h0[:, :], h1T_hi_made)
            for g in range(K, 2 * K):
                high_w0(g)
            act.wait_ge(first_input_done, 1)
            high_x(0, 1)
            high_w1(wx, w1_raw[0], "wx")
            slots(act, slot, T)

        @block.vector
        def _(dve):
            def low_part(lo, whole, hi, done):
                nc.vector.tensor_tensor(lo, whole, hi.bitcast(F32), ALU.subtract).then_inc(done, 1)

            def turn_quadrants(dst, src, done):
                nc.vector.transpose(dst.rearrange("p (c b r) -> p r c b", c=K, r=NQ),
                                    src.rearrange("p r (f c) -> p r c f", c=K)).then_inc(done, 1)

            def low_w1(w, raw, n, pairs):
                for i in pairs:
                    dve.wait_ge(w1_hi_made, n + i + 1)
                    low_part(w[1][:, 2 * i:2 * i + 2, :], raw[:, 2 * i:2 * i + 2, :], w[0][:, 2 * i:2 * i + 2, :],
                             w1_lo_made)

            def turn_x(q, j):
                if j % CH == 0:
                    dve.wait_ge(xq_loaded[j // CH % 2], (q + j // RING + 1) * NQ * DMA_INC)
                turn_quadrants(xT[:, j % 2, :], xq[:, j // CH % 2, :, j % CH, :], x_turned)

            def low_x(q, j):
                dve.wait_ge(xT_hi_made, q * RING + j + 1)
                low_part(xT_lo[:, :], xT[:, j % 2, :], xT_hi[:, :], xT_lo_made)

            def turn_h1(n):
                dve.wait_ge(h1_spread, n * NQ * DMA_INC)
                turn_quadrants(h1T[:, :], h1q[:, :].rearrange("p (r f) -> p r f", r=NQ), h1_turned)

            def low_h1(n, whole):
                dve.wait_ge(h1T_hi_made, n + 1)
                low_part(h1T_lo[:, :], whole, h1T_hi[:, :], h1T_lo_made)

            def slot(q, j):
                s = q * RING + j
                if before(T, q, j):
                    dve.wait_ge(acc0_done, s + 1)
                    nc.vector.tensor_tensor(pre0[:, :], acc0[j % 2][:, :], bias0[:, :],
                                            ALU.add).then_inc(pre0_made, 1)
                if from_on(1, q, j) and before(T - 1, q, j):
                    low_x(q, j + 1)
                if before(T, q, j):
                    dve.wait_ge(gate_made, s + 1)
                    if j % CH == 0:
                        dve.wait_ge(x_loaded[j // CH % 2], (q + j // RING + 1) * DMA_INC)
                    nc.vector.tensor_tensor(gated[:, :], gate[:, :], xs[:, j % RING, :],
                                            ALU.mult).then_inc(gated_made, 1)
                    dve.wait_ge(gated_made, s + 1)
                    dve.wait_ge(leaked_made, s + 1)
                    nc.vector.tensor_tensor(arg0[:, :], leaked[:, :], gated[:, :],
                                            ALU.add).then_inc(arg0_made, 1)
                if not from_on(1, q, j):
                    low_w1(wx, w1_raw[0], 0, range(1))
                if from_on(2, q, j):
                    if before(T, q, j):
                        turn_h1(s - 1)
                    low_h1(s - 1, h1T[:, :] if before(T, q, j) else turn_h0[:, :])
                if before(T, q, j):
                    dve.wait_ge(h0T_hi_made, s + 2)
                    low_part(h0T_lo[:, :], turn_h0[:, :], h0T_hi[:, :], h0T_lo_made)
                    nc.vector.tensor_tensor(x1T[:, :], turn_h0[:, :], xT[:, j % 2, :],
                                            ALU.add).then_inc(x1T_made, 1)
                if not from_on(1, q, j):
                    low_w1(wx, w1_raw[0], 0, range(1, K // 2))
                if from_on(1, q, j):
                    dve.wait_ge(acc1_done, s)
                    nc.vector.tensor_tensor(pre1[:, :], acc1[(j - 1) % 2][:, :], bias1[:, :],
                                            ALU.add).then_inc(pre1_made, 1)
                if before(T, q, j):
                    dve.wait_ge(x1T_hi_made, s + 1)
                    low_part(x1T_lo[:, :], x1T[:, :], x1T_hi[:, :], x1T_lo_made)
                if before(T - 2, q, j):
                    turn_x(q, j + 2)
                if not from_on(1, q, j):
                    low_w1(wh1, w1_raw[1], K // 2, range(K // 2))
                if not before(T, q, j):
                    dve.wait_ge(x1_made, s)
                    dve.wait_ge(h1_made, s)
                    nc.vector.tensor_tensor(outs[:, (j - 1) % RING, :], x1[:, (j - 1) % 2, :],
                                            h1[:, (j - 1) % 2, :], ALU.add).then_inc(last_out_made, 1)

            def low_w0(g):
                dve.wait_ge(w0_hi_made, g + 1)
                low_part((wh0 if g // K else wz)[1][:, g % K, :], turn_w[g % len(turn_w)][:, :],
                         (wh0 if g // K else wz)[0][:, g % K, :], w0_lo_made)

            for g in range(K):
                low_w0(g)
                if g == 1:
                    turn_x(0, 0)
            low_x(0, 0)
            turn_x(0, 1)
            dve.wait_ge(h1T_hi_made, 1)
            low_part(h0T_lo[:, :], turn_h0[:, :], h0T_hi[:, :], h0T_lo_made)
            low_part(h1T_lo[:, :], turn_h0[:, :], h1T_hi[:, :], h1T_lo_made)
            for g in range(K, 2 * K):
                low_w0(g)
            dve.wait_ge(vec_loaded, 3 * DMA_INC)
            nc.vector.tensor_scalar(leak[:, :], leak[:, :], -1.0, 1.0, ALU.mult, ALU.add).then_inc(leak_ready, 1)
            low_x(0, 1)
            slots(dve, slot, T)

        @block.gpsimd
        def _(pool):
            nc.gpsimd.memset(ident[:, :], 0.0).then_inc(ident_zeroed, 1)
            pool.wait_ge(ident_zeroed, 1)
            nc.gpsimd.affine_select(out=ident[:, :], in_=ident[:, :], compare_op=ALU.not_equal, fill=1.0,
                                    base=0, pattern=[[-1, P]], channel_multiplier=1).then_inc(ident_ready, 1)
            pool.wait_ge(cond_loaded, DMA_INC)
            pool.wait_ge(leak_ready, 1)
            nc.gpsimd.tensor_tensor(leaked[:, :], h_init[:, :], leak[:, :], ALU.mult).then_inc(leaked_made, 1)

            def slot(q, j):
                s = q * RING + j
                pool.wait_ge(h0_made, s + 1)
                if j % CH == 0:
                    pool.wait_ge(x_loaded[j // CH % 2], (q + j // RING + 1) * DMA_INC)
                if from_on(2, q, j):
                    pool.wait_ge(out_made, s - 1)
                nc.gpsimd.tensor_tensor(x1[:, j % 2, :], xs[:, j % RING, :], h0[:, j % 2, :],
                                        ALU.add).then_inc(x1_made, 1)
                if before(T - 1, q, j):
                    nc.gpsimd.tensor_tensor(leaked[:, :], h0[:, j % 2, :], leak[:, :],
                                            ALU.mult).then_inc(leaked_made, 1)
                if from_on(1, q, j):
                    m = j - 1
                    pool.wait_ge(h1_made, s)
                    pool.wait_ge(x1_made, s)
                    if m % CH == 0 and from_on(2 * CH, q, m):
                        pool.wait_ge(stored[m // CH % 2], (q + m // RING) * DMA_INC)
                    nc.gpsimd.tensor_tensor(outs[:, m % RING, :], x1[:, m % 2, :], h1[:, m % 2, :],
                                            ALU.add).then_inc(out_made, 1)

            slots(pool, slot, T - 1)


_INS = ["x", "cond_1024", "L0_cond_W", "L0_cond_b", "L0_cond_alpha", "L1_cond_Wx", "L1_cond_Wh", "L1_cond_b"]


def kernel(**inputs):
    import numpy as _np
    import concourse.bacc as _bacc
    from concourse import mybir as _mybir
    from concourse.bass_utils import run_bass_kernel_spmd as _run

    nc = _bacc.Bacc("TRN2", target_bir_lowering=False, num_devices=1)
    arrays, args = {}, []
    for name in _INS:
        a = _np.ascontiguousarray(inputs[name])
        arrays[f"in_{name}_dram"] = a
        args.append(nc.dram_tensor(f"in_{name}_dram", a.shape, _mybir.dt.from_np(a.dtype),
                                   kind="ExternalInput").ap())
    args.append(nc.dram_tensor("out_dram", inputs["x"].shape, _mybir.dt.float32, kind="ExternalOutput").ap())
    cond_recurrences(nc, *args)
    r = _run(nc, [arrays], core_ids=[0])
    return r.results[0]["out_dram"]
```
